# Optimizing a Trainium2 kernel written in Bass

```python
import numpy as np
import jax
import jax.numpy as jnp

def _softmax(x, axis=-1):
    return jax.nn.softmax(x, axis=axis)

def _gelu(x):
    return jax.nn.gelu(x, approximate=True)

def _silu(x):
    return jax.nn.silu(x)

def _sigmoid(x):
    return jax.nn.sigmoid(x)

def _layernorm(x, axis=-1, eps=1e-05):
    m = jnp.mean(x, axis=axis, keepdims=True)
    v = jnp.var(x, axis=axis, keepdims=True)
    return (x - m) / jnp.sqrt(v + eps)

def _scatter_add(tgt, idx, src, axis=0):
    return tgt.at[idx].add(src)

def _segment_sum(src, seg, n):
    return jax.ops.segment_sum(src, seg, n)
kernel_name = 'mk_rec_standalone_d1_rec_r8_4c93f6'

def setup_inputs(seed: int=0):
    np.random.seed(seed)
    _w = jnp.asarray

    def _rec_inputs():
        import jax
        import jax.numpy as jnp
        _rk = jax.random.key(seed)
        r_x = jax.random.bernoulli(jax.random.fold_in(_rk, 1), 0.0009984, (1024, 10202)).astype(jnp.float32)
        return r_x
    r_x = _rec_inputs()

    def _L0_rec_setup():
        import jax, jax.numpy as jnp
        import numpy as np
        VOCAB = 10202
        DIM = 32
        BATCH = 512
        key = jax.random.key(seed)
        k1, k2 = jax.random.split(key)
        x = (jax.random.uniform(k1, (BATCH, VOCAB), dtype=jnp.float32) < 0.001).astype(jnp.float32)
        w = jax.random.normal(k2, (VOCAB, DIM), dtype=jnp.float32) * 0.05
        b = jnp.zeros((DIM,), dtype=jnp.float32)
        return {'x': x, 'w': w, 'b': b}
    _L0_rec_all = _L0_rec_setup()
    _L0_rec_in = {k: v for k, v in _L0_rec_all.items() if k in ('w', 'b')}
    del _L0_rec_all
    return {'r_x': r_x, 'L0_rec_w': _L0_rec_in['w'], 'L0_rec_b': _L0_rec_in['b']}

def reference(r_x, L0_rec_w, L0_rec_b):
    import jax
    import jax.numpy as jnp

    def _L0_rec_ref(x, w, b):
        import jax, jax.numpy as jnp
        import numpy as np
        VOCAB = 10202
        DIM = 32
        BATCH = 512
        h = jax.nn.sigmoid(x @ w + b)
        y_pred = jax.nn.sigmoid(h @ w.T)
        return y_pred
    y = _L0_rec_ref(r_x, L0_rec_w, L0_rec_b)
    return y

_drawn_inputs = setup_inputs


def setup_inputs(seed=0):
    import zlib

    import numpy as np

    out = dict(_drawn_inputs(seed))
    spreads = {'L0_rec_b': (0.0, 2.0)}
    factors = {'r_x': 8.0}
    for name, (base, spread) in spreads.items():
        noise = np.random.default_rng([zlib.crc32(name.encode()), seed]).standard_normal(out[name].shape)
        drawn = base * np.exp(spread * noise) if base else spread * noise
        out[name] = jnp.asarray(drawn.astype(out[name].dtype))
    for name, factor in factors.items():
        out[name] = (out[name] * factor).astype(out[name].dtype)
    return out
```

```python
import concourse.bass as bass
from concourse import mybir
from contextlib import ExitStack


def rec_autoencoder(nc: bass.Bass, x: bass.AP, w: bass.AP, b: bass.AP, y: bass.AP):
    f32 = mybir.dt.float32
    bf16 = mybir.dt.bfloat16
    ALU = mybir.AluOpType
    ACT = mybir.ActivationFunctionType

    ROWS, V = x.shape
    D = w.shape[1]
    P = 128
    GROUPS = P // D
    TILES = ROWS // P
    BLOCKS = -(-V // P)
    LAST = V - (BLOCKS - 1) * P
    ROUND = 4
    ROUNDS = BLOCKS // ROUND
    CHUNK_ROUNDS = 4
    CHUNK = CHUNK_ROUNDS * ROUND * P
    CHUNKS = ROUNDS // CHUNK_ROUNDS
    BANK = 512
    PAIR = 2 * BANK
    PAIRS = -(-V // PAIR)
    STACKED = 3
    BEHIND = 3
    LAG = 2
    TURNED = 4
    FILL = 8
    FILLS = BLOCKS // FILL
    assert V > (PAIRS - 1) * PAIR and BLOCKS % (ROUND * CHUNK_ROUNDS) == 0 and ROUNDS == 2 * PAIRS

    x_tiles = x.rearrange("(t p) v -> t p v", p=P)
    y_tiles = y.rearrange("(t p) v -> t p v", p=P)

    def chunk_cols(c):
        return slice(c * CHUNK, min(V, (c + 1) * CHUNK))

    def pair_cols(k):
        return slice(k * PAIR, min(V, (k + 1) * PAIR))

    ctx = ExitStack()
    with ctx:
        def sb(name, shape, dt=f32):
            return ctx.enter_context(nc.sbuf_tensor(name, shape, dt))

        def pb(name, shape):
            return ctx.enter_context(nc.psum_tensor(name, shape, f32))

        def sem(name):
            return ctx.enter_context(nc.semaphore(name))

        x_sb = sb("x_sb", [P, 2 * CHUNKS, CHUNK])
        y_sb = sb("y_sb", [P, PAIRS, PAIR])
        w_sb = sb("w_sb", [P, BLOCKS, D])
        stack_a = sb("stack_a", [P, BLOCKS * P], bf16)
        stack_b = sb("stack_b", [P, BLOCKS * P], bf16)
        turned = sb("turned", [P, TURNED, ROUND * P])
        quarters = sb("quarters", [P, P])
        h_sb = sb("h_sb", [P, 2, P])
        h_rest = sb("h_rest", [P, P])
        h_mid = sb("h_mid", [P, P], bf16)
        h_a = sb("h_a", [P, 2, P], bf16)
        h_b = sb("h_b", [P, 2, P], bf16)
        bias = sb("bias", [P, 1])
        warm = sb("warm", [1, 1])
        ident = sb("ident", [P, P])
        ident_bf = sb("ident_bf", [P, P], bf16)
        same_d = sb("same_d", [P, P])

        parts = y_sb[:, :, :].rearrange("p a b -> p (a b)").bitcast(bf16)
        part_a = parts[:, 0:BLOCKS * P].rearrange("p (c g d) -> p c g d", g=GROUPS, d=D)
        part_b = parts[:, BLOCKS * P:2 * BLOCKS * P].rearrange("p (c g d) -> p c g d", g=GROUPS, d=D)
        w_rest = stack_b[:, 0:2 * BLOCKS * D].bitcast(f32).rearrange("p (c d) -> p c d", d=D)

        turn_ps = [pb(f"turn_ps{i}", [P, BANK]) for i in range(2)]
        sum_ps = [pb(f"sum_ps{i}", [P, BANK]) for i in range(2)]
        logit_ps = [pb(f"logit_ps{i}", [P, PAIR]) for i in range(2)]

        w_loaded = sem("w_loaded")
        w_padded = sem("w_padded")
        bias_loaded = sem("bias_loaded")
        x_loaded = [sem(f"x_loaded{i}") for i in range(2 * CHUNKS)]
        consts_ready = sem("consts_ready")
        pool_step = sem("pool_step")
        part1_ready = sem("part1_ready")
        rest_ready = sem("rest_ready")
        part2_ready = sem("part2_ready")
        part3_ready = sem("part3_ready")
        part_act = sem("part_act")
        w_turned = sem("w_turned")
        w_stacked_dve = sem("w_stacked_dve")
        w_stacked_act = sem("w_stacked_act")
        round_turned = sem("round_turned")
        round_copied = sem("round_copied")
        round_summed = sem("round_summed")
        quarters_copied = sem("quarters_copied")
        sum_ready = sem("sum_ready")
        h_ready = sem("h_ready")
        h_split = sem("h_split")
        logits_ready = sem("logits_ready")
        probs_ready = sem("probs_ready")
        stored = [sem(f"stored{i}") for i in range(PAIRS)]

        def fill_bank(f):
            return logit_ps[f // 2 % 2][:, :].bitcast(bf16)[:, f % 2 * FILL * P:(f % 2 + 1) * FILL * P]

        def fill_stack(f):
            stack = stack_a if f < FILLS else stack_b
            return stack[:, f % FILLS * FILL * P:(f % FILLS + 1) * FILL * P]

        def fills_after(t, r):
            at = PAIRS * t + r // 2 - BEHIND
            return [2 * at, 2 * at + 1] if r % 2 and 0 <= at < FILLS else []

        block = ctx.enter_context(nc.Block())

        @block.sync
        def _(sp):
            def load(t, parity, c):
                cols = chunk_cols(c)
                slot = parity * CHUNKS + c
                sp.dma_start(x_sb[:, slot, 0:cols.stop - cols.start],
                             x_tiles[t, :, cols]).then_inc(x_loaded[slot], 16)

            def store(t, k):
                cols = pair_cols(k)
                sp.wait_ge(probs_ready, PAIRS * t + k + 1)
                sp.dma_start(y_tiles[t, :, cols],
                             y_sb[:, k, 0:cols.stop - cols.start]).then_inc(stored[k], 16)

            def tile_step(t, parity, loads, stores, late_stores):
                for r in range(ROUNDS):
                    if loads and r % CHUNK_ROUNDS == CHUNK_ROUNDS - 1:
                        sp.wait_ge(round_turned, ROUNDS * t + r + 1)
                        load(t + 2, parity, r // CHUNK_ROUNDS)
                    if r % 2:
                        k = r // 2
                        if k < BEHIND and late_stores:
                            store(t - 2, PAIRS - BEHIND + k)
                        if k >= BEHIND and stores:
                            store(t - 1, k - BEHIND)

            sp.wait_ge(w_padded, 1)
            sp.dma_start(w_sb[:, 0:BLOCKS - 1, :],
                         w[0:(BLOCKS - 1) * P, :].rearrange("(c p) d -> p c d", p=P)).then_inc(w_loaded, 16)
            sp.dma_start(w_sb[0:LAST, BLOCKS - 1, :], w[(BLOCKS - 1) * P:V, :]).then_inc(w_loaded, 16)
            for c in range(CHUNKS):
                load(0, 0, c)
            for g in range(GROUPS):
                sp.dma_start(bias[g * D:(g + 1) * D, 0:1], b.rearrange("(d o) -> d o", o=1)).then_inc(bias_loaded, 16)
            for c in range(CHUNKS):
                load(1, 1, c)
            tile_step(0, 0, True, False, False)
            tile_step(1, 1, True, True, False)
            with sp.Fori(0, (TILES - 4) // 2) as i:
                for e in range(2):
                    tile_step(2 * i + 2 + e, e, True, True, True)
            for t in range(TILES - 2, TILES):
                tile_step(t, t % 2, False, True, True)
            for k in range(BEHIND):
                store(TILES - 2, PAIRS - BEHIND + k)
            for k in range(PAIRS):
                store(TILES - 1, k)
            for k in range(PAIRS):
                sp.wait_ge(stored[k], 16 * TILES)

        @block.gpsimd
        def _(pool):
            steps = [0]

            def step(ins):
                steps[0] += 1
                ins.then_inc(pool_step, 1)
                pool.wait_ge(pool_step, steps[0])

            nc.gpsimd.memset(w_sb[:, BLOCKS - 1, :], 0.0).then_inc(w_padded, 1)
            step(nc.gpsimd.memset(ident[:, :], 0.0))
            step(nc.gpsimd.affine_select(out=ident[:, :], in_=ident[:, :], compare_op=ALU.not_equal, fill=1.0,
                                         base=0, pattern=[[-1, P]], channel_multiplier=1))
            nc.gpsimd.tensor_copy(ident_bf[:, :], ident[:, :])
            step(nc.gpsimd.memset(same_d[:, :], 0.0))
            for g in range(GROUPS):
                v = same_d[:, :].rearrange("p (g d) -> p g d", d=D)
                ins = nc.gpsimd.affine_select(out=v, in_=v, compare_op=ALU.not_equal, fill=1.0,
                                              base=-g * D, pattern=[[0, GROUPS], [-1, D]], channel_multiplier=1)
                if g < GROUPS - 1:
                    step(ins)
            ins.then_inc(consts_ready, 1)

            pool.wait_ge(part2_ready, 1)
            nc.gpsimd.tensor_tensor(part_b[:, :, 0, :], w_rest, part_a[:, :, 1, :], ALU.subtract).then_inc(part3_ready, 1)

            def split_h(t, parity, n, reuse):
                c = [0]

                def then(ins):
                    c[0] += 1
                    ins.then_inc(pool_step, 1)
                    pool.wait_ge(pool_step, n + c[0])

                a, bb, h = h_a[:, parity, :], h_b[:, parity, :], h_sb[:, parity, :]
                pool.wait_ge(h_ready, t + 1)
                if reuse:
                    pool.wait_ge(logits_ready, PAIRS * (t - 1))
                then(nc.gpsimd.tensor_copy(a, h))
                then(nc.gpsimd.tensor_tensor(h_rest[:, :], h, a, ALU.subtract))
                then(nc.gpsimd.tensor_copy(h_mid[:, :], h_rest[:, :]))
                then(nc.gpsimd.tensor_tensor(bb, h_rest[:, :], h_mid[:, :], ALU.subtract))
                nc.gpsimd.tensor_copy(bb[0:D], a[0:D]).then_inc(h_split, 1)
                nc.gpsimd.tensor_copy(bb[2 * D:3 * D], h_mid[2 * D:3 * D, :]).then_inc(h_split, 1)
                nc.gpsimd.tensor_copy(a[2 * D:4 * D], h_mid[2 * D:4 * D, :]).then_inc(h_split, 1)

            STEPS = 4
            base = steps[0]
            for t in range(TILES):
                split_h(t, t % 2, base + STEPS * t, t >= 2)

        @block.scalar
        def _(act):
            def decode(t, k, first):
                cols = pair_cols(k)
                n = cols.stop - cols.start
                act.wait_ge(logits_ready, PAIRS * t + k + 1)
                if not first:
                    act.wait_ge(stored[k], 16 * t)
                nc.scalar.activation(y_sb[:, k, 0:n], logit_ps[k % 2][:, 0:n],
                                     ACT.Sigmoid).then_inc(probs_ready, 1)

            def encode(t, parity, reuse):
                act.wait_ge(sum_ready, t + 1)
                if reuse:
                    act.wait_ge(h_split, STACKED * (t - 1))
                nc.scalar.activation(h_sb[:, parity, :], sum_ps[parity][:, 0:P], ACT.Sigmoid,
                                     bias=bias[:, 0:1]).then_inc(h_ready, 1)

            def fill(f):
                act.wait_ge(w_turned, f + 1)
                nc.scalar.copy(fill_stack(f), fill_bank(f)).then_inc(w_stacked_act, 1)

            def tile_step(t, parity, decodes, late_decodes):
                for k in range(PAIRS):
                    if k == 1:
                        encode(t - 1, parity, late_decodes)
                    if k < BEHIND and late_decodes:
                        decode(t - 2, PAIRS - BEHIND + k, False)
                    if k >= BEHIND and decodes:
                        decode(t - 1, k - BEHIND, not late_decodes)

            act.wait_ge(consts_ready, 1)
            nc.scalar.activation(warm[0:1, 0:1], ident[0:1, 0:1], ACT.Sigmoid)
            act.wait_ge(w_loaded, 32)
            nc.scalar.copy(part_a[:, :, 2, :], w_sb[:, :, :]).then_inc(part_act, 1)
            nc.scalar.copy(part_b[:, :, 1, :], w_sb[:, :, :]).then_inc(part_act, 1)
            act.wait_ge(rest_ready, 1)
            nc.scalar.copy(part_a[:, :, 3, :], w_rest).then_inc(part_act, 1)
            nc.scalar.copy(part_b[:, :, 3, :], w_rest).then_inc(part_act, 1)
            act.wait_ge(part3_ready, 1)
            nc.scalar.copy(part_b[:, :, 2, :], part_b[:, :, 0, :]).then_inc(part_act, 1)
            for f in range(1, 2 * FILLS, 2):
                fill(f)
            act.wait_ge(bias_loaded, 16 * GROUPS)
            for k in range(PAIRS):
                if k == 1:
                    encode(0, 0, False)
                if k >= BEHIND:
                    decode(0, k - BEHIND, True)
            for k in range(PAIRS):
                if k == 1:
                    encode(1, 1, False)
                if k < BEHIND:
                    decode(0, PAIRS - BEHIND + k, True)
                else:
                    decode(1, k - BEHIND, False)
            with act.Fori(0, (TILES - 4) // 2) as i:
                for e in range(2):
                    tile_step(2 * i + 3 + e, e, True, True)
            for t in (TILES - 1,):
                tile_step(t, (t - 1) % 2, True, True)
            decode(TILES - 2, PAIRS - BEHIND, False)
            encode(TILES - 1, (TILES - 1) % 2, True)
            for k in range(PAIRS - BEHIND + 1, PAIRS):
                decode(TILES - 2, k, False)
            for k in range(PAIRS):
                decode(TILES - 1, k, False)

        @block.vector
        def _(dve):
            def copy_round(t, r, first):
                slot = r % TURNED
                dve.wait_ge(round_turned, ROUNDS * t + r + 1)
                if not (first and r < TURNED):
                    dve.wait_ge(round_summed, ROUNDS * t + r + 1 - TURNED)
                if r < ROUNDS - 1:
                    nc.vector.tensor_copy(turned[:, slot, :], turn_ps[r % 2][:, :]).then_inc(round_copied, 1)
                else:
                    full = (ROUND - 1) * P
                    nc.vector.tensor_copy(turned[:, slot, 0:full], turn_ps[r % 2][:, 0:full])
                    nc.vector.tensor_copy(turned[0:LAST, slot, full:], turn_ps[r % 2][0:LAST, full:]).then_inc(round_copied, 1)

            def copy_quarters(t, parity, first):
                dve.wait_ge(round_summed, ROUNDS * (t + 1))
                if not first:
                    dve.wait_ge(sum_ready, t)
                nc.vector.tensor_copy(quarters[:, :], sum_ps[parity][:, 0:P]).then_inc(quarters_copied, 1)

            def tile_step(t, parity, first):
                for r in range(ROUNDS):
                    copy_round(t, r, False)
                    if r == LAG - 1:
                        copy_quarters(t - 1, 1 - parity, first)

            def fill(f):
                dve.wait_ge(w_turned, f + 1)
                nc.vector.tensor_copy(fill_stack(f), fill_bank(f)).then_inc(w_stacked_dve, 1)

            dve.wait_ge(w_loaded, 32)
            nc.vector.tensor_copy(part_a[:, :, 0, :], w_sb[:, :, :]).then_inc(part1_ready, 1)
            dve.wait_ge(part1_ready, 1)
            nc.vector.tensor_tensor(w_rest, w_sb[:, :, :], part_a[:, :, 0, :], ALU.subtract).then_inc(rest_ready, 1)
            for r in range(ROUNDS):
                copy_round(0, r, True)
                if r == 1:
                    dve.wait_ge(rest_ready, 1)
                    nc.vector.tensor_copy(part_a[:, :, 1, :], w_rest).then_inc(part2_ready, 1)
                for f in fills_after(0, r)[0:1]:
                    fill(f)
            for r in range(ROUNDS):
                copy_round(1, r, False)
                if r == LAG - 1:
                    copy_quarters(0, 0, True)
                for f in fills_after(1, r)[0:1]:
                    fill(f)
            with dve.Fori(0, (TILES - 2) // 2) as i:
                for e in range(2):
                    tile_step(2 * i + 2 + e, e, False)
            copy_quarters(TILES - 1, (TILES - 1) % 2, False)

        @block.tensor
        def _(pe):
            def turn(t, parity, r):
                bank = turn_ps[r % 2]
                slot = parity * CHUNKS + r // CHUNK_ROUNDS
                for j in range(ROUND):
                    at = (r % CHUNK_ROUNDS * ROUND + j) * P
                    n = P if (r, j) != (ROUNDS - 1, ROUND - 1) else LAST
                    ins = nc.tensor.transpose(bank[0:n, j * P:(j + 1) * P], x_sb[:, slot, at:at + n], ident[:, :])
                ins.then_inc(round_turned, 1)

            def add_round(parity, r):
                for j in range(ROUND):
                    n = P if (r, j) != (ROUNDS - 1, ROUND - 1) else LAST
                    ins = nc.tensor.matmul(sum_ps[parity][j * D:(j + 1) * D, 0:P], w_sb[0:n, ROUND * r + j, :],
                                           turned[0:n, r % TURNED, j * P:(j + 1) * P],
                                           start=(r == 0), stop=(r == ROUNDS - 1))
                ins.then_inc(round_summed, 1)

            def add_quarters(t, parity):
                pe.wait_ge(quarters_copied, t + 1)
                nc.tensor.matmul(sum_ps[parity][:, 0:P], same_d[:, :], quarters[:, :],
                                 start=True, stop=True).then_inc(sum_ready, 1)

            def decode(t, parity, k, free):
                if k == 0:
                    pe.wait_ge(h_split, STACKED * (t + 1))
                if free:
                    pe.wait_ge(probs_ready, PAIRS * t + k - 1)
                cols = pair_cols(k)
                for at in range(cols.start, cols.stop, BANK):
                    n = min(BANK, cols.stop - at)
                    out = logit_ps[k % 2][:, at - cols.start:at - cols.start + n]
                    nc.tensor.matmul(out, h_a[:, parity, :], stack_a[:, at:at + n], start=True, stop=False)
                    ins = nc.tensor.matmul(out, h_b[:, parity, :], stack_b[:, at:at + n], start=False, stop=True)
                ins.then_inc(logits_ready, 1)

            def fill(f):
                if f == 0:
                    pe.wait_ge(part_act, 3)
                    pe.wait_ge(part2_ready, 1)
                if f == FILLS:
                    pe.wait_ge(part_act, 5)
                    pe.wait_ge(part3_ready, 1)
                if f >= 4:
                    pe.wait_ge(w_stacked_act if f % 2 else w_stacked_dve, f // 2 - 1)
                part = part_a if f < FILLS else part_b
                for j in range(FILL):
                    lhs = part[:, f % FILLS * FILL + j, :, :].rearrange("p g d -> p (g d)")
                    ins = nc.tensor.transpose(fill_bank(f)[:, j * P:(j + 1) * P], lhs, ident_bf[:, :])
                ins.then_inc(w_turned, 1)

            def round_step(t, parity, use, r, started, reuse):
                if r % CHUNK_ROUNDS == 0:
                    pe.wait_ge(x_loaded[parity * CHUNKS + r // CHUNK_ROUNDS], 16 * use)
                if started or r >= LAG:
                    pe.wait_ge(round_copied, ROUNDS * t + r + 1 - LAG)
                turn(t, parity, r)
                if r >= LAG:
                    if r == LAG and reuse:
                        pe.wait_ge(h_ready, t - 1)
                    add_round(parity, r - LAG)
                elif started:
                    add_round(1 - parity, ROUNDS - LAG + r)
                if r == LAG + 1 and started:
                    add_quarters(t - 1, 1 - parity)

            pe.wait_ge(consts_ready, 1)
            for r in range(ROUNDS):
                if r == LAG:
                    pe.wait_ge(w_loaded, 32)
                round_step(0, 0, 1, r, False, False)
                for f in fills_after(0, r):
                    fill(f)
            for r in range(ROUNDS):
                round_step(1, 1, 1, r, True, False)
                for f in fills_after(1, r):
                    fill(f)
                if r % 2 and r // 2 >= BEHIND:
                    if r // 2 == BEHIND:
                        pe.wait_ge(w_stacked_dve, FILLS)
                        pe.wait_ge(w_stacked_act, FILLS)
                    decode(0, 0, r // 2 - BEHIND, r // 2 - BEHIND >= 2)
            with pe.Fori(0, (TILES - 2) // 2) as i:
                for e in range(2):
                    t = 2 * i + 2 + e
                    for r in range(ROUNDS):
                        round_step(t, e, i + 2, r, True, True)
                        if r % 2 and r // 2 < BEHIND:
                            decode(t - 2, e, PAIRS - BEHIND + r // 2, True)
                        if r % 2 and r // 2 >= BEHIND:
                            decode(t - 1, 1 - e, r // 2 - BEHIND, True)
            last = (TILES - 1) % 2
            pe.wait_ge(round_copied, ROUNDS * TILES)
            for r in range(ROUNDS - LAG, ROUNDS):
                add_round(last, r)
            decode(TILES - 2, 1 - last, PAIRS - BEHIND, True)
            add_quarters(TILES - 1, last)
            for k in range(PAIRS - BEHIND + 1, PAIRS):
                decode(TILES - 2, 1 - last, k, True)
            for k in range(PAIRS):
                decode(TILES - 1, last, k, True)


_INS = ['r_x', 'L0_rec_w', 'L0_rec_b']


def kernel(**inputs):
    import numpy as _np
    import concourse.bacc as _bacc
    from concourse import mybir as _mybir
    from concourse.bass_utils import run_bass_kernel_spmd as _run

    nc = _bacc.Bacc("TRN2", target_bir_lowering=False, num_devices=1)
    arrays, args = {}, []
    for name in _INS:
        a = _np.ascontiguousarray(inputs[name])
        arrays[f"in_{name}_dram"] = a
        args.append(nc.dram_tensor(f"in_{name}_dram", a.shape, _mybir.dt.from_np(a.dtype), kind="ExternalInput").ap())
    shape = inputs['r_x'].shape
    args.append(nc.dram_tensor("out_0_dram", shape, _mybir.dt.float32, kind="ExternalOutput").ap())
    rec_autoencoder(nc, *args)
    r = _run(nc, [arrays], core_ids=[0])
    return r.results[0]["out_0_dram"]
```

```python
import concourse.bass as bass
from concourse import mybir
from contextlib import ExitStack


def rec_autoencoder(nc: bass.Bass, x: bass.AP, w: bass.AP, b: bass.AP, y: bass.AP):
    f32 = mybir.dt.float32
    f32r = mybir.dt.float32r
    ALU = mybir.AluOpType
    ACT = mybir.ActivationFunctionType

    ROWS, V = x.shape
    D = w.shape[1]
    P = 128
    GROUPS = P // D
    TILES = ROWS // P
    BLOCKS = -(-V // P)
    LAST = V - (BLOCKS - 1) * P
    ROUND = 4
    ROUNDS = BLOCKS // ROUND
    CHUNK_ROUNDS = 4
    CHUNK = CHUNK_ROUNDS * ROUND * P
    CHUNKS = ROUNDS // CHUNK_ROUNDS
    BANK = 512
    PAIR = 2 * BANK
    PAIRS = -(-V // PAIR)
    BEHIND = 3
    LAG = 2
    SPLIT_AT = 4
    H_COPIES = 2
    TURNED = 4
    FILLS = BLOCKS // ROUND
    FILL_FROM = 6
    assert V > (PAIRS - 1) * PAIR and BLOCKS % (ROUND * CHUNK_ROUNDS) == 0 and ROUNDS == 2 * PAIRS

    x_tiles = x.rearrange("(t p) v -> t p v", p=P)
    y_tiles = y.rearrange("(t p) v -> t p v", p=P)

    def chunk_cols(c):
        return slice(c * CHUNK, min(V, (c + 1) * CHUNK))

    def pair_cols(k):
        return slice(k * PAIR, min(V, (k + 1) * PAIR))

    ctx = ExitStack()
    with ctx:
        def sb(name, shape, dt=f32):
            return ctx.enter_context(nc.sbuf_tensor(name, shape, dt))

        def pb(name, shape):
            return ctx.enter_context(nc.psum_tensor(name, shape, f32))

        def sem(name):
            return ctx.enter_context(nc.semaphore(name))

        x_sb = sb("x_sb", [P, 2 * CHUNKS, CHUNK])
        y_sb = sb("y_sb", [P, CHUNKS, CHUNK])
        w_sb = sb("w_sb", [P, BLOCKS, D])
        w_stack = sb("w_stack", [P, BLOCKS * P], f32r)
        turned = sb("turned", [P, TURNED, ROUND * P])
        quarters = sb("quarters", [P, P])
        h_sb = sb("h_sb", [P, 2, P])
        h_stack = sb("h_stack", [P, 2, P], f32r)
        bias = sb("bias", [P, 1])
        warm = sb("warm", [1, 1])
        ident = sb("ident", [P, P])
        same_d = sb("same_d", [P, P])

        parts = y_sb[:, :, :].rearrange("p a b -> p (a b)").rearrange("p (c g d) -> p c g d", g=GROUPS, d=D)

        turn_ps = [pb(f"turn_ps{i}", [P, BANK]) for i in range(2)]
        sum_ps = [pb(f"sum_ps{i}", [P, BANK]) for i in range(2)]
        logit_ps = [pb(f"logit_ps{i}", [P, PAIR]) for i in range(2)]

        w_loaded = sem("w_loaded")
        w_padded = sem("w_padded")
        bias_loaded = sem("bias_loaded")
        consts_ready = sem("consts_ready")
        pool_step = sem("pool_step")
        part_rounded = sem("part_rounded")
        part_left = sem("part_left")
        parts_copied = sem("parts_copied")
        w_turned = sem("w_turned")
        w_stacked_dve = sem("w_stacked_dve")
        w_stacked_act = sem("w_stacked_act")
        x_loaded = [sem(f"x_loaded{i}") for i in range(2 * CHUNKS)]
        round_turned = sem("round_turned")
        round_copied = sem("round_copied")
        round_summed = sem("round_summed")
        quarters_copied = sem("quarters_copied")
        sum_ready = sem("sum_ready")
        h_ready = sem("h_ready")
        h_split = sem("h_split")
        logits_ready = sem("logits_ready")
        probs_ready = sem("probs_ready")
        stored = [sem(f"stored{i}") for i in range(CHUNKS)]

        def fill_bank(f):
            return logit_ps[f // 2 % 2][:, f % 2 * BANK:(f % 2 + 1) * BANK]

        def fill_stack(f):
            return w_stack[:, f * BANK:(f + 1) * BANK]

        def fills_after(t, r):
            at = ROUNDS * t + r - FILL_FROM - 1
            return [at, at + 1] if at % 2 == 0 and 0 <= at < FILLS else []

        block = ctx.enter_context(nc.Block())

        @block.sync
        def _(sp):
            def load(t, parity, c):
                cols = chunk_cols(c)
                slot = parity * CHUNKS + c
                sp.dma_start(x_sb[:, slot, 0:cols.stop - cols.start],
                             x_tiles[t, :, cols]).then_inc(x_loaded[slot], 16)

            def store(t, k):
                if k % 2:
                    cols = chunk_cols(k // 2)
                    sp.wait_ge(probs_ready, PAIRS * t + k + 1)
                    sp.dma_start(y_tiles[t, :, cols],
                                 y_sb[:, k // 2, 0:cols.stop - cols.start]).then_inc(stored[k // 2], 16)

            def tile_step(t, parity, loads, stores, late_stores):
                for r in range(ROUNDS):
                    if loads and r % CHUNK_ROUNDS == CHUNK_ROUNDS - 1:
                        sp.wait_ge(round_turned, ROUNDS * t + r + 1)
                        load(t + 2, parity, r // CHUNK_ROUNDS)
                    if r % 2:
                        k = r // 2
                        if k < BEHIND and late_stores:
                            store(t - 2, PAIRS - BEHIND + k)
                        if k >= BEHIND and stores:
                            store(t - 1, k - BEHIND)

            for t in range(2):
                for c in range(CHUNKS):
                    load(t, t, c)
            tile_step(0, 0, True, False, False)
            tile_step(1, 1, True, True, False)
            with sp.Fori(0, (TILES - 4) // 2) as i:
                for e in range(2):
                    tile_step(2 * i + 2 + e, e, True, True, True)
            for t in range(TILES - 2, TILES):
                tile_step(t, t % 2, False, True, True)
            for k in range(BEHIND):
                store(TILES - 2, PAIRS - BEHIND + k)
            for k in range(PAIRS):
                store(TILES - 1, k)
            for c in range(CHUNKS):
                sp.wait_ge(stored[c], 16 * TILES)

        @block.gpsimd
        def _(pool):
            steps = [0]

            def step(ins):
                steps[0] += 1
                ins.then_inc(pool_step, 1)
                pool.wait_ge(pool_step, steps[0])

            nc.gpsimd.memset(w_sb[:, BLOCKS - 1, :], 0.0).then_inc(w_padded, 1)
            step(nc.gpsimd.memset(ident[:, :], 0.0))
            step(nc.gpsimd.affine_select(out=ident[:, :], in_=ident[:, :], compare_op=ALU.not_equal, fill=1.0,
                                         base=0, pattern=[[-1, P]], channel_multiplier=1))
            step(nc.gpsimd.memset(same_d[:, :], 0.0))
            for g in range(GROUPS):
                v = same_d[:, :].rearrange("p (g d) -> p g d", d=D)
                ins = nc.gpsimd.affine_select(out=v, in_=v, compare_op=ALU.not_equal, fill=1.0,
                                              base=-g * D, pattern=[[0, GROUPS], [-1, D]], channel_multiplier=1)
                if g < GROUPS - 1:
                    step(ins)
            ins.then_inc(consts_ready, 1)

        @block.scalar
        def _(act):
            def decode(t, k, first):
                cols = pair_cols(k)
                n = cols.stop - cols.start
                act.wait_ge(logits_ready, PAIRS * t + k + 1)
                if not first and k % 2 == 0:
                    act.wait_ge(stored[k // 2], 16 * t)
                at = k % 2 * PAIR
                nc.scalar.activation(y_sb[:, k // 2, at:at + n], logit_ps[k % 2][:, 0:n],
                                     ACT.Sigmoid).then_inc(probs_ready, 1)

            def encode(t, parity):
                act.wait_ge(sum_ready, t + 1)
                for out in (h_sb, h_stack):
                    nc.scalar.activation(out[:, parity, :], sum_ps[parity][:, 0:P], ACT.Sigmoid,
                                         bias=bias[:, 0:1]).then_inc(h_ready, 1)

            def fill(f):
                act.wait_ge(w_turned, f + 1)
                nc.scalar.copy(fill_stack(f), fill_bank(f)).then_inc(w_stacked_act, 1)

            def tile_step(t, parity):
                for k in range(PAIRS):
                    if k == 1:
                        encode(t - 1, parity)
                    if k < BEHIND:
                        decode(t - 2, PAIRS - BEHIND + k, False)
                    else:
                        decode(t - 1, k - BEHIND, False)

            act.dma_start(w_sb[:, 0:BLOCKS - 1, :],
                          w[0:(BLOCKS - 1) * P, :].rearrange("(c p) d -> p c d", p=P)).then_inc(w_loaded, 16)
            act.wait_ge(w_padded, 1)
            act.dma_start(w_sb[0:LAST, BLOCKS - 1, :], w[(BLOCKS - 1) * P:V, :]).then_inc(w_loaded, 16)
            for g in range(GROUPS):
                act.dma_start(bias[g * D:(g + 1) * D, 0:1], b.rearrange("(d o) -> d o", o=1)).then_inc(bias_loaded, 16)
            act.wait_ge(consts_ready, 1)
            nc.scalar.activation(warm[0:1, 0:1], ident[0:1, 0:1], ACT.Sigmoid)
            act.wait_ge(part_rounded, 1)
            nc.scalar.copy(parts[:, :, 2, :], parts[:, :, 0, :]).then_inc(parts_copied, 1)
            act.wait_ge(part_left, 1)
            nc.scalar.copy(parts[:, :, 3, :], parts[:, :, 1, :]).then_inc(parts_copied, 1)
            for r in range(ROUNDS):
                for f in fills_after(0, r)[1:]:
                    fill(f)
            for k in range(PAIRS):
                if k == 1:
                    act.wait_ge(bias_loaded, 16 * GROUPS)
                    encode(0, 0)
                for f in fills_after(1, 2 * k + 1)[1:]:
                    fill(f)
                if k >= BEHIND:
                    decode(0, k - BEHIND, True)
            for k in range(PAIRS):
                if k == 1:
                    encode(1, 1)
                if k < BEHIND:
                    decode(0, PAIRS - BEHIND + k, True)
                else:
                    decode(1, k - BEHIND, False)
            with act.Fori(0, (TILES - 4) // 2) as i:
                for e in range(2):
                    tile_step(2 * i + 3 + e, e)
            tile_step(TILES - 1, TILES % 2)
            decode(TILES - 2, PAIRS - BEHIND, False)
            encode(TILES - 1, (TILES - 1) % 2)
            for k in range(PAIRS - BEHIND + 1, PAIRS):
                decode(TILES - 2, k, False)
            for k in range(PAIRS):
                decode(TILES - 1, k, False)

        @block.vector
        def _(dve):
            def copy_round(t, r, first):
                slot = r % TURNED
                dve.wait_ge(round_turned, ROUNDS * t + r + 1)
                if not (first and r < TURNED):
                    dve.wait_ge(round_summed, ROUNDS * t + r + 1 - TURNED)
                if r < ROUNDS - 1:
                    nc.vector.tensor_copy(turned[:, slot, :], turn_ps[r % 2][:, :]).then_inc(round_copied, 1)
                else:
                    full = (ROUND - 1) * P
                    nc.vector.tensor_copy(turned[:, slot, 0:full], turn_ps[r % 2][:, 0:full])
                    nc.vector.tensor_copy(turned[0:LAST, slot, full:],
                                          turn_ps[r % 2][0:LAST, full:]).then_inc(round_copied, 1)

            def copy_quarters(t, parity, first):
                dve.wait_ge(round_summed, ROUNDS * (t + 1))
                if not first:
                    dve.wait_ge(sum_ready, t)
                nc.vector.tensor_copy(quarters[:, :], sum_ps[parity][:, 0:P]).then_inc(quarters_copied, 1)

            def split_h(t, parity):
                dve.wait_ge(h_ready, H_COPIES * (t + 1))
                low = h_stack[2 * D:4 * D, parity, :]
                nc.vector.tensor_tensor(low, h_sb[2 * D:4 * D, parity, :], low.bitcast(f32),
                                        ALU.subtract).then_inc(h_split, 1)

            def tile_step(t, parity, first):
                for r in range(ROUNDS):
                    copy_round(t, r, False)
                    if r == LAG - 1:
                        copy_quarters(t - 1, 1 - parity, first)
                    if r == SPLIT_AT:
                        split_h(t - 1, 1 - parity)

            def fill(f):
                dve.wait_ge(w_turned, f + 1)
                nc.vector.tensor_copy(fill_stack(f), fill_bank(f)).then_inc(w_stacked_dve, 1)

            for r in range(ROUNDS):
                copy_round(0, r, True)
                if r == LAG - 1:
                    dve.wait_ge(w_loaded, 32)
                    nc.vector.tensor_copy(parts[:, :, 0, :].bitcast(f32r), w_sb[:, :, :]).then_inc(part_rounded, 1)
                    dve.wait_ge(part_rounded, 1)
                    nc.vector.tensor_tensor(parts[:, :, 1, :], w_sb[:, :, :], parts[:, :, 0, :],
                                            ALU.subtract).then_inc(part_left, 1)
                for f in fills_after(0, r)[0:1]:
                    fill(f)
            for r in range(ROUNDS):
                copy_round(1, r, False)
                if r == LAG - 1:
                    copy_quarters(0, 0, True)
                if r == SPLIT_AT:
                    split_h(0, 0)
                for f in fills_after(1, r)[0:1]:
                    fill(f)
            with dve.Fori(0, (TILES - 2) // 2) as i:
                for e in range(2):
                    tile_step(2 * i + 2 + e, e, False)
            copy_quarters(TILES - 1, (TILES - 1) % 2, False)
            split_h(TILES - 1, (TILES - 1) % 2)

        @block.tensor
        def _(pe):
            def turn(t, parity, r):
                bank = turn_ps[r % 2]
                slot = parity * CHUNKS + r // CHUNK_ROUNDS
                for j in range(ROUND):
                    at = (r % CHUNK_ROUNDS * ROUND + j) * P
                    n = P if (r, j) != (ROUNDS - 1, ROUND - 1) else LAST
                    ins = nc.tensor.transpose(bank[0:n, j * P:(j + 1) * P], x_sb[:, slot, at:at + n], ident[:, :])
                ins.then_inc(round_turned, 1)

            def add_round(parity, r):
                for j in range(ROUND):
                    n = P if (r, j) != (ROUNDS - 1, ROUND - 1) else LAST
                    ins = nc.tensor.matmul(sum_ps[parity][j * D:(j + 1) * D, 0:P], w_sb[0:n, ROUND * r + j, :],
                                           turned[0:n, r % TURNED, j * P:(j + 1) * P],
                                           start=(r == 0), stop=(r == ROUNDS - 1))
                ins.then_inc(round_summed, 1)

            def add_quarters(t, parity):
                pe.wait_ge(quarters_copied, t + 1)
                nc.tensor.matmul(sum_ps[parity][:, 0:P], same_d[:, :], quarters[:, :],
                                 start=True, stop=True).then_inc(sum_ready, 1)

            def decode(t, parity, k, free):
                if k == 0:
                    pe.wait_ge(h_split, t + 1)
                if free:
                    pe.wait_ge(probs_ready, PAIRS * t + k - 1)
                cols = pair_cols(k)
                for at in range(cols.start, cols.stop, BANK):
                    n = min(BANK, cols.stop - at)
                    out = logit_ps[k % 2][:, at - cols.start:at - cols.start + n]
                    ins = nc.tensor.matmul(out, h_stack[:, parity, :], w_stack[:, at:at + n], start=True, stop=True)
                ins.then_inc(logits_ready, 1)

            def fill(f):
                if f == 0:
                    pe.wait_ge(part_left, 1)
                    pe.wait_ge(parts_copied, 2)
                if f >= 4:
                    pe.wait_ge(w_stacked_act if f % 2 else w_stacked_dve, f // 2 - 1)
                for j in range(ROUND):
                    lhs = parts[:, f * ROUND + j, :, :].rearrange("p g d -> p (g d)")
                    ins = nc.tensor.transpose(fill_bank(f)[:, j * P:(j + 1) * P], lhs, ident[:, :])
                ins.then_inc(w_turned, 1)

            def round_step(t, parity, use, r, started, reuse):
                if r % CHUNK_ROUNDS == 0:
                    pe.wait_ge(x_loaded[parity * CHUNKS + r // CHUNK_ROUNDS], 16 * use)
                if started or r >= LAG:
                    pe.wait_ge(round_copied, ROUNDS * t + r + 1 - LAG)
                turn(t, parity, r)
                if r >= LAG:
                    if r == LAG and reuse:
                        pe.wait_ge(h_ready, H_COPIES * (t - 1))
                    add_round(parity, r - LAG)
                elif started:
                    add_round(1 - parity, ROUNDS - LAG + r)
                if r == LAG + 1 and started:
                    add_quarters(t - 1, 1 - parity)

            pe.wait_ge(consts_ready, 1)
            for r in range(ROUNDS):
                if r == LAG:
                    pe.wait_ge(w_loaded, 32)
                round_step(0, 0, 1, r, False, False)
                for f in fills_after(0, r):
                    fill(f)
            for r in range(ROUNDS):
                round_step(1, 1, 1, r, True, False)
                for f in fills_after(1, r):
                    fill(f)
                if r % 2 and r // 2 >= BEHIND:
                    if r // 2 == BEHIND:
                        pe.wait_ge(w_stacked_dve, FILLS // 2)
                        pe.wait_ge(w_stacked_act, FILLS // 2)
                    decode(0, 0, r // 2 - BEHIND, r // 2 - BEHIND >= 2)
            with pe.Fori(0, (TILES - 2) // 2) as i:
                for e in range(2):
                    t = 2 * i + 2 + e
                    for r in range(ROUNDS):
                        round_step(t, e, i + 2, r, True, True)
                        if r % 2 and r // 2 < BEHIND:
                            decode(t - 2, e, PAIRS - BEHIND + r // 2, True)
                        if r % 2 and r // 2 >= BEHIND:
                            decode(t - 1, 1 - e, r // 2 - BEHIND, True)
            last = (TILES - 1) % 2
            pe.wait_ge(round_copied, ROUNDS * TILES)
            for r in range(ROUNDS - LAG, ROUNDS):
                add_round(last, r)
            decode(TILES - 2, 1 - last, PAIRS - BEHIND, True)
            add_quarters(TILES - 1, last)
            for k in range(PAIRS - BEHIND + 1, PAIRS):
                decode(TILES - 2, 1 - last, k, True)
            for k in range(PAIRS):
                decode(TILES - 1, last, k, True)


_INS = ['r_x', 'L0_rec_w', 'L0_rec_b']


def kernel(**inputs):
    import numpy as _np
    import concourse.bacc as _bacc
    from concourse import mybir as _mybir
    from concourse.bass_utils import run_bass_kernel_spmd as _run

    nc = _bacc.Bacc("TRN2", target_bir_lowering=False, num_devices=1)
    arrays, args = {}, []
    for name in _INS:
        a = _np.ascontiguousarray(inputs[name])
        arrays[f"in_{name}_dram"] = a
        args.append(nc.dram_tensor(f"in_{name}_dram", a.shape, _mybir.dt.from_np(a.dtype), kind="ExternalInput").ap())
    shape = inputs['r_x'].shape
    args.append(nc.dram_tensor("out_0_dram", shape, _mybir.dt.float32, kind="ExternalOutput").ap())
    rec_autoencoder(nc, *args)
    r = _run(nc, [arrays], core_ids=[0])
    return r.results[0]["out_0_dram"]
```

```python
import concourse.bass as bass
from concourse import mybir
from contextlib import ExitStack


def rec_autoencoder(nc: bass.Bass, x: bass.AP, w: bass.AP, b: bass.AP, y: bass.AP):
    f32 = mybir.dt.float32
    f32r = mybir.dt.float32r
    ALU = mybir.AluOpType
    ACT = mybir.ActivationFunctionType

    ROWS, V = x.shape
    D = w.shape[1]
    P = 128
    GROUPS = P // D
    TILES = ROWS // P
    BLOCKS = -(-V // P)
    LAST = V - (BLOCKS - 1) * P
    ROUND = 4
    ROUNDS = BLOCKS // ROUND
    CHUNK_ROUNDS = 4
    CHUNK = CHUNK_ROUNDS * ROUND * P
    CHUNKS = ROUNDS // CHUNK_ROUNDS
    BANK = 512
    PAIR = 2 * BANK
    PAIRS = -(-V // PAIR)
    BEHIND = 3
    LAG = 2
    SPLIT_AT = 4
    H_COPIES = 2
    TURNED = 4
    FILLS = BLOCKS // ROUND
    HALVES = 2
    FILL_FROM = 6
    assert V > (PAIRS - 1) * PAIR and BLOCKS % (ROUND * CHUNK_ROUNDS) == 0 and ROUNDS == 2 * PAIRS

    x_tiles = x.rearrange("(t p) v -> t p v", p=P)
    y_tiles = y.rearrange("(t p) v -> t p v", p=P)

    def chunk_cols(c):
        return slice(c * CHUNK, min(V, (c + 1) * CHUNK))

    def pair_cols(k):
        return slice(k * PAIR, min(V, (k + 1) * PAIR))

    ctx = ExitStack()
    with ctx:
        def sb(name, shape, dt=f32):
            return ctx.enter_context(nc.sbuf_tensor(name, shape, dt))

        def pb(name, shape):
            return ctx.enter_context(nc.psum_tensor(name, shape, f32))

        def sem(name):
            return ctx.enter_context(nc.semaphore(name))

        x_sb = sb("x_sb", [P, 2 * CHUNKS, CHUNK])
        y_sb = sb("y_sb", [P, CHUNKS, CHUNK])
        w_sb = sb("w_sb", [P, BLOCKS, D])
        w_stack = sb("w_stack", [P, BLOCKS * P], f32r)
        turned = sb("turned", [P, TURNED, ROUND * P])
        quarters = sb("quarters", [P, P])
        h_sb = sb("h_sb", [P, 2, P])
        h_stack = sb("h_stack", [P, 2, P], f32r)
        bias = sb("bias", [P, 1])
        warm = sb("warm", [1, 1])
        ident = sb("ident", [P, P])
        same_d = sb("same_d", [P, P])

        w_raw = w_sb[:, :, :].rearrange("p (m e) d -> p m (e d)", e=ROUND)
        w_half_turned = y_sb[:, :, :].rearrange("p a b -> p (a b)")[:, 0:BLOCKS * D].rearrange(
            "k (m q) -> k m q", q=P)
        parts = y_sb[:, :, :].rearrange("p a b -> p (a b)").rearrange("p (c g d) -> p c g d", g=GROUPS, d=D)

        turn_ps = [pb(f"turn_ps{i}", [P, BANK]) for i in range(2)]
        sum_ps = [pb(f"sum_ps{i}", [P, BANK]) for i in range(2)]
        logit_ps = [pb(f"logit_ps{i}", [P, PAIR]) for i in range(2)]

        w_loaded = sem("w_loaded")
        w_padded = sem("w_padded")
        w_half_ready = sem("w_half_ready")
        w_blocks_turned = sem("w_blocks_turned")
        w_blocks_ready = sem("w_blocks_ready")
        bias_loaded = sem("bias_loaded")
        consts_ready = sem("consts_ready")
        pool_step = sem("pool_step")
        part_rounded = sem("part_rounded")
        part_left = sem("part_left")
        parts_copied = sem("parts_copied")
        w_turned = sem("w_turned")
        w_stacked_dve = sem("w_stacked_dve")
        w_stacked_act = sem("w_stacked_act")
        x_loaded = [sem(f"x_loaded{i}") for i in range(2 * CHUNKS)]
        round_turned = sem("round_turned")
        round_copied = sem("round_copied")
        round_summed = sem("round_summed")
        quarters_copied = sem("quarters_copied")
        sum_ready = sem("sum_ready")
        h_ready = sem("h_ready")
        h_split = sem("h_split")
        logits_ready = sem("logits_ready")
        probs_ready = sem("probs_ready")
        stored = [sem(f"stored{i}") for i in range(CHUNKS)]

        def half(i):
            return slice(i * BLOCKS // HALVES, (i + 1) * BLOCKS // HALVES)

        def fill_bank(f):
            return logit_ps[f // 2 % 2][:, f % 2 * BANK:(f % 2 + 1) * BANK]

        def fill_stack(f):
            return w_stack[:, f * BANK:(f + 1) * BANK]

        def fills_after(t, r):
            at = ROUNDS * t + r - FILL_FROM - 1
            return [at, at + 1] if at % 2 == 0 and 0 <= at < FILLS else []

        whole = (ROUNDS - 1) * ROUND * P
        quads = (V - whole) // ROUND
        spread = quads // 16 * 16
        left = V - whole - quads * ROUND
        w_loads = [
            (w_raw[:, 0:ROUNDS - 1, :], w[0:whole, :].rearrange("(m p e) d -> p m (e d)", p=P, e=ROUND)),
            (w_raw[0:spread, ROUNDS - 1, :],
             w[whole:whole + spread * ROUND, :].rearrange("(p e) d -> p (e d)", e=ROUND)),
            (w_raw[spread:quads, ROUNDS - 1, :],
             w[whole + spread * ROUND:V - left, :].rearrange("(p e) d -> p (e d)", e=ROUND)),
            (w_raw[quads:quads + 1, ROUNDS - 1, 0:left * D],
             w[V - left:V, :].rearrange("(p e) d -> p (e d)", e=left)),
        ]
        W_LOADS = len(w_loads)
        SHARE = BANK // P
        SHARES = ROUNDS // SHARE

        block = ctx.enter_context(nc.Block())

        @block.sync
        def _(sp):
            def load(t, parity, c):
                cols = chunk_cols(c)
                slot = parity * CHUNKS + c
                sp.dma_start(x_sb[:, slot, 0:cols.stop - cols.start],
                             x_tiles[t, :, cols]).then_inc(x_loaded[slot], 16)

            def store(t, k):
                if k % 2:
                    cols = chunk_cols(k // 2)
                    sp.wait_ge(probs_ready, PAIRS * t + k + 1)
                    sp.dma_start(y_tiles[t, :, cols],
                                 y_sb[:, k // 2, 0:cols.stop - cols.start]).then_inc(stored[k // 2], 16)

            def tile_step(t, parity, loads, stores, late_stores):
                for r in range(ROUNDS):
                    if loads and r % CHUNK_ROUNDS == CHUNK_ROUNDS - 1:
                        sp.wait_ge(round_turned, ROUNDS * t + r + 1)
                        load(t + 2, parity, r // CHUNK_ROUNDS)
                    if r % 2:
                        k = r // 2
                        if k < BEHIND and late_stores:
                            store(t - 2, PAIRS - BEHIND + k)
                        if k >= BEHIND and stores:
                            store(t - 1, k - BEHIND)

            for n, (to, rows) in enumerate(w_loads):
                if n == 1:
                    sp.wait_ge(w_padded, 1)
                sp.dma_start(to, rows).then_inc(w_loaded, 16)
            for t in range(2):
                for c in range(CHUNKS):
                    load(t, t, c)
            tile_step(0, 0, True, False, False)
            tile_step(1, 1, True, True, False)
            with sp.Fori(0, (TILES - 4) // 2) as i:
                for e in range(2):
                    tile_step(2 * i + 2 + e, e, True, True, True)
            for t in range(TILES - 2, TILES):
                tile_step(t, t % 2, False, True, True)
            for k in range(BEHIND):
                store(TILES - 2, PAIRS - BEHIND + k)
            for k in range(PAIRS):
                store(TILES - 1, k)
            for c in range(CHUNKS):
                sp.wait_ge(stored[c], 16 * TILES)

        @block.gpsimd
        def _(pool):
            steps = [0]

            def step(ins):
                steps[0] += 1
                ins.then_inc(pool_step, 1)
                pool.wait_ge(pool_step, steps[0])

            nc.gpsimd.memset(w_raw[:, ROUNDS - 1, :], 0.0).then_inc(w_padded, 1)
            step(nc.gpsimd.memset(ident[:, :], 0.0))
            step(nc.gpsimd.affine_select(out=ident[:, :], in_=ident[:, :], compare_op=ALU.not_equal, fill=1.0,
                                         base=0, pattern=[[-1, P]], channel_multiplier=1))
            step(nc.gpsimd.memset(same_d[:, :], 0.0))
            for g in range(GROUPS):
                v = same_d[:, :].rearrange("p (g d) -> p g d", d=D)
                ins = nc.gpsimd.affine_select(out=v, in_=v, compare_op=ALU.not_equal, fill=1.0,
                                              base=-g * D, pattern=[[0, GROUPS], [-1, D]], channel_multiplier=1)
                if g < GROUPS - 1:
                    step(ins)
            ins.then_inc(consts_ready, 1)

        @block.scalar
        def _(act):
            def decode(t, k, first):
                cols = pair_cols(k)
                n = cols.stop - cols.start
                act.wait_ge(logits_ready, PAIRS * t + k + 1)
                if not first and k % 2 == 0:
                    act.wait_ge(stored[k // 2], 16 * t)
                at = k % 2 * PAIR
                nc.scalar.activation(y_sb[:, k // 2, at:at + n], logit_ps[k % 2][:, 0:n],
                                     ACT.Sigmoid).then_inc(probs_ready, 1)

            def encode(t, parity):
                act.wait_ge(sum_ready, t + 1)
                for out in (h_sb, h_stack):
                    nc.scalar.activation(out[:, parity, :], sum_ps[parity][:, 0:P], ACT.Sigmoid,
                                         bias=bias[:, 0:1]).then_inc(h_ready, 1)

            def fill(f):
                act.wait_ge(w_turned, f + 1)
                nc.scalar.copy(fill_stack(f), fill_bank(f)).then_inc(w_stacked_act, 1)

            def tile_step(t, parity):
                for k in range(PAIRS):
                    if k == 1:
                        encode(t - 1, parity)
                    if k < BEHIND:
                        decode(t - 2, PAIRS - BEHIND + k, False)
                    else:
                        decode(t - 1, k - BEHIND, False)

            for g in range(GROUPS):
                act.dma_start(bias[g * D:(g + 1) * D, 0:1], b.rearrange("(d o) -> d o", o=1)).then_inc(bias_loaded, 16)
            act.wait_ge(consts_ready, 1)
            nc.scalar.activation(warm[0:1, 0:1], ident[0:1, 0:1], ACT.Sigmoid)
            for n in range(SHARES):
                act.wait_ge(w_blocks_turned, n + 1)
                nc.scalar.copy(w_sb[:, n * SHARE * ROUND:(n + 1) * SHARE * ROUND, :],
                               fill_bank(n).rearrange("q (c d) -> q c d", d=D)).then_inc(w_blocks_ready, 1)
            for i in range(HALVES):
                act.wait_ge(part_rounded, i + 1)
                nc.scalar.copy(parts[:, half(i), 2, :], parts[:, half(i), 0, :]).then_inc(parts_copied, 1)
                act.wait_ge(part_left, i + 1)
                nc.scalar.copy(parts[:, half(i), 3, :], parts[:, half(i), 1, :]).then_inc(parts_copied, 1)
            for r in range(ROUNDS):
                for f in fills_after(0, r)[1:]:
                    fill(f)
            for k in range(PAIRS):
                if k == 1:
                    act.wait_ge(bias_loaded, 16 * GROUPS)
                    encode(0, 0)
                for f in fills_after(1, 2 * k + 1)[1:]:
                    fill(f)
                if k >= BEHIND:
                    decode(0, k - BEHIND, True)
            for k in range(PAIRS):
                if k == 1:
                    encode(1, 1)
                if k < BEHIND:
                    decode(0, PAIRS - BEHIND + k, True)
                else:
                    decode(1, k - BEHIND, False)
            with act.Fori(0, (TILES - 4) // 2) as i:
                for e in range(2):
                    tile_step(2 * i + 3 + e, e)
            tile_step(TILES - 1, TILES % 2)
            decode(TILES - 2, PAIRS - BEHIND, False)
            encode(TILES - 1, (TILES - 1) % 2)
            for k in range(PAIRS - BEHIND + 1, PAIRS):
                decode(TILES - 2, k, False)
            for k in range(PAIRS):
                decode(TILES - 1, k, False)

        @block.vector
        def _(dve):
            def copy_round(t, r, first):
                slot = r % TURNED
                dve.wait_ge(round_turned, ROUNDS * t + r + 1)
                if not (first and r < TURNED):
                    dve.wait_ge(round_summed, ROUNDS * t + r + 1 - TURNED)
                if r < ROUNDS - 1:
                    nc.vector.tensor_copy(turned[:, slot, :], turn_ps[r % 2][:, :]).then_inc(round_copied, 1)
                else:
                    full = (ROUND - 1) * P
                    nc.vector.tensor_copy(turned[:, slot, 0:full], turn_ps[r % 2][:, 0:full])
                    nc.vector.tensor_copy(turned[0:LAST, slot, full:],
                                          turn_ps[r % 2][0:LAST, full:]).then_inc(round_copied, 1)

            def copy_quarters(t, parity, first):
                dve.wait_ge(round_summed, ROUNDS * (t + 1))
                if not first:
                    dve.wait_ge(sum_ready, t)
                nc.vector.tensor_copy(quarters[:, :], sum_ps[parity][:, 0:P]).then_inc(quarters_copied, 1)

            def split_h(t, parity):
                dve.wait_ge(h_ready, H_COPIES * (t + 1))
                low = h_stack[2 * D:4 * D, parity, :]
                nc.vector.tensor_tensor(low, h_sb[2 * D:4 * D, parity, :], low.bitcast(f32),
                                        ALU.subtract).then_inc(h_split, 1)

            def tile_step(t, parity, first):
                for r in range(ROUNDS):
                    copy_round(t, r, False)
                    if r == LAG - 1:
                        copy_quarters(t - 1, 1 - parity, first)
                    if r == SPLIT_AT:
                        split_h(t - 1, 1 - parity)

            def fill(f):
                dve.wait_ge(w_turned, f + 1)
                nc.vector.tensor_copy(fill_stack(f), fill_bank(f)).then_inc(w_stacked_dve, 1)

            def split_w(i, step):
                high = parts[:, half(i), 0, :]
                if step == 0:
                    dve.wait_ge(w_blocks_ready, SHARES)
                    nc.vector.tensor_copy(high.bitcast(f32r), w_sb[:, half(i), :]).then_inc(part_rounded, 1)
                else:
                    dve.wait_ge(part_rounded, i + 1)
                    nc.vector.tensor_tensor(parts[:, half(i), 1, :], w_sb[:, half(i), :], high,
                                            ALU.subtract).then_inc(part_left, 1)

            dve.wait_ge(w_loaded, 16 * W_LOADS)
            for n in range(SHARES):
                ms = slice(n * SHARE, (n + 1) * SHARE)
                nc.vector.transpose(w_half_turned[:, ms, :].rearrange("k m (q e) -> k m e q", e=ROUND),
                                    w_raw[:, ms, :].rearrange("p m (e d) -> p m e d", d=D)
                                    ).then_inc(w_half_ready, 1)
            for r in range(ROUNDS):
                copy_round(0, r, True)
                if r < 2 * HALVES:
                    split_w(r // 2, r % 2)
                for f in fills_after(0, r)[0:1]:
                    fill(f)
            for r in range(ROUNDS):
                copy_round(1, r, False)
                if r == LAG - 1:
                    copy_quarters(0, 0, True)
                if r == SPLIT_AT:
                    split_h(0, 0)
                for f in fills_after(1, r)[0:1]:
                    fill(f)
            with dve.Fori(0, (TILES - 2) // 2) as i:
                for e in range(2):
                    tile_step(2 * i + 2 + e, e, False)
            copy_quarters(TILES - 1, (TILES - 1) % 2, False)
            split_h(TILES - 1, (TILES - 1) % 2)

        @block.tensor
        def _(pe):
            def turn(t, parity, r):
                bank = turn_ps[r % 2]
                slot = parity * CHUNKS + r // CHUNK_ROUNDS
                for j in range(ROUND):
                    at = (r % CHUNK_ROUNDS * ROUND + j) * P
                    n = P if (r, j) != (ROUNDS - 1, ROUND - 1) else LAST
                    ins = nc.tensor.transpose(bank[0:n, j * P:(j + 1) * P], x_sb[:, slot, at:at + n], ident[:, :])
                ins.then_inc(round_turned, 1)

            def add_round(parity, r):
                for j in range(ROUND):
                    n = P if (r, j) != (ROUNDS - 1, ROUND - 1) else LAST
                    ins = nc.tensor.matmul(sum_ps[parity][j * D:(j + 1) * D, 0:P], w_sb[0:n, ROUND * r + j, :],
                                           turned[0:n, r % TURNED, j * P:(j + 1) * P],
                                           start=(r == 0), stop=(r == ROUNDS - 1))
                ins.then_inc(round_summed, 1)

            def add_quarters(t, parity):
                pe.wait_ge(quarters_copied, t + 1)
                nc.tensor.matmul(sum_ps[parity][:, 0:P], same_d[:, :], quarters[:, :],
                                 start=True, stop=True).then_inc(sum_ready, 1)

            def decode(t, parity, k, free):
                if k == 0:
                    pe.wait_ge(h_split, t + 1)
                if free:
                    pe.wait_ge(probs_ready, PAIRS * t + k - 1)
                cols = pair_cols(k)
                for at in range(cols.start, cols.stop, BANK):
                    n = min(BANK, cols.stop - at)
                    out = logit_ps[k % 2][:, at - cols.start:at - cols.start + n]
                    ins = nc.tensor.matmul(out, h_stack[:, parity, :], w_stack[:, at:at + n], start=True, stop=True)
                ins.then_inc(logits_ready, 1)

            def turn_w_blocks():
                for n in range(SHARES):
                    pe.wait_ge(w_half_ready, n + 1)
                    if n >= 4:
                        pe.wait_ge(w_blocks_ready, n - 3)
                    for j in range(SHARE):
                        ins = nc.tensor.transpose(fill_bank(n)[:, j * P:(j + 1) * P],
                                                  w_half_turned[:, n * SHARE + j, :], ident[:, :])
                    ins.then_inc(w_blocks_turned, 1)

            def fill(f):
                if f == 0:
                    pe.wait_ge(part_left, HALVES)
                    pe.wait_ge(parts_copied, 2 * HALVES)
                if f >= 4:
                    pe.wait_ge(w_stacked_act if f % 2 else w_stacked_dve, f // 2 - 1)
                for j in range(ROUND):
                    lhs = parts[:, f * ROUND + j, :, :].rearrange("p g d -> p (g d)")
                    ins = nc.tensor.transpose(fill_bank(f)[:, j * P:(j + 1) * P], lhs, ident[:, :])
                ins.then_inc(w_turned, 1)

            def round_step(t, parity, use, r, started, reuse):
                if r % CHUNK_ROUNDS == 0:
                    pe.wait_ge(x_loaded[parity * CHUNKS + r // CHUNK_ROUNDS], 16 * use)
                if started or r >= LAG:
                    pe.wait_ge(round_copied, ROUNDS * t + r + 1 - LAG)
                turn(t, parity, r)
                if r >= LAG:
                    if r == LAG and reuse:
                        pe.wait_ge(h_ready, H_COPIES * (t - 1))
                    add_round(parity, r - LAG)
                elif started:
                    add_round(1 - parity, ROUNDS - LAG + r)
                if r == LAG + 1 and started:
                    add_quarters(t - 1, 1 - parity)

            pe.wait_ge(consts_ready, 1)
            turn_w_blocks()
            for r in range(ROUNDS):
                if r == LAG:
                    pe.wait_ge(w_blocks_ready, SHARES)
                round_step(0, 0, 1, r, False, False)
                for f in fills_after(0, r):
                    fill(f)
            for r in range(ROUNDS):
                round_step(1, 1, 1, r, True, False)
                for f in fills_after(1, r):
                    fill(f)
                if r % 2 and r // 2 >= BEHIND:
                    if r // 2 == BEHIND:
                        pe.wait_ge(w_stacked_dve, FILLS // 2)
                        pe.wait_ge(w_stacked_act, FILLS // 2)
                    decode(0, 0, r // 2 - BEHIND, r // 2 - BEHIND >= 2)
            with pe.Fori(0, (TILES - 2) // 2) as i:
                for e in range(2):
                    t = 2 * i + 2 + e
                    for r in range(ROUNDS):
                        round_step(t, e, i + 2, r, True, True)
                        if r % 2 and r // 2 < BEHIND:
                            decode(t - 2, e, PAIRS - BEHIND + r // 2, True)
                        if r % 2 and r // 2 >= BEHIND:
                            decode(t - 1, 1 - e, r // 2 - BEHIND, True)
            last = (TILES - 1) % 2
            pe.wait_ge(round_copied, ROUNDS * TILES)
            for r in range(ROUNDS - LAG, ROUNDS):
                add_round(last, r)
            decode(TILES - 2, 1 - last, PAIRS - BEHIND, True)
            add_quarters(TILES - 1, last)
            for k in range(PAIRS - BEHIND + 1, PAIRS):
                decode(TILES - 2, 1 - last, k, True)
            for k in range(PAIRS):
                decode(TILES - 1, last, k, True)


_INS = ['r_x', 'L0_rec_w', 'L0_rec_b']


def kernel(**inputs):
    import numpy as _np
    import concourse.bacc as _bacc
    from concourse import mybir as _mybir
    from concourse.bass_utils import run_bass_kernel_spmd as _run

    nc = _bacc.Bacc("TRN2", target_bir_lowering=False, num_devices=1)
    arrays, args = {}, []
    for name in _INS:
        a = _np.ascontiguousarray(inputs[name])
        arrays[f"in_{name}_dram"] = a
        args.append(nc.dram_tensor(f"in_{name}_dram", a.shape, _mybir.dt.from_np(a.dtype), kind="ExternalInput").ap())
    shape = inputs['r_x'].shape
    args.append(nc.dram_tensor("out_0_dram", shape, _mybir.dt.float32, kind="ExternalOutput").ap())
    rec_autoencoder(nc, *args)
    r = _run(nc, [arrays], core_ids=[0])
    return r.results[0]["out_0_dram"]
```
